# Optimizing a Trainium2 kernel written in Bass

```python
import numpy as np
import jax
import jax.numpy as jnp

def _softmax(x, axis=-1):
    return jax.nn.softmax(x, axis=axis)

def _gelu(x):
    return jax.nn.gelu(x, approximate=True)

def _silu(x):
    return jax.nn.silu(x)

def _sigmoid(x):
    return jax.nn.sigmoid(x)

def _layernorm(x, axis=-1, eps=1e-05):
    m = jnp.mean(x, axis=axis, keepdims=True)
    v = jnp.var(x, axis=axis, keepdims=True)
    return (x - m) / jnp.sqrt(v + eps)

def _scatter_add(tgt, idx, src, axis=0):
    return tgt.at[idx].add(src)

def _segment_sum(src, seg, n):
    return jax.ops.segment_sum(src, seg, n)
kernel_name = 'mk_seq_postln_d1_jaxref_r4_bb8813'

def setup_inputs(seed: int=0):
    np.random.seed(seed)
    _w = jnp.asarray

    def _L0_attn_setup():
        import jax, jax.numpy as jnp
        import numpy as np
        B, L, D, H, F = (2, 256, 256, 16, 1024)
        DH = D // H
        EPS = 1e-06

        def _layernorm(x, g, b, eps=1e-05):
            m = jnp.mean(x, axis=-1, keepdims=True)
            v = jnp.mean((x - m) ** 2, axis=-1, keepdims=True)
            return (x - m) / jnp.sqrt(v + eps) * g + b

        def _decoder_layer(inputs, Wq, bq, Wk, bk, Wv, bv, Wo, bo, ln1_g, ln1_b, W1, b1, W2, b2, ln2_g, ln2_b):
            Bn, Ln, Dn = inputs.shape

            def heads(W, b):
                return (inputs @ W + b).reshape(Bn, Ln, H, DH).transpose(0, 2, 1, 3)
            q = jax.nn.sigmoid(heads(Wq, bq))
            k = jax.nn.sigmoid(heads(Wk, bk))
            v = heads(Wv, bv)
            normal = (jnp.arange(Ln, dtype=jnp.float32) + 1.0)[None, None, :]
            sink_in = normal / jnp.einsum('bhld,bhld->bhl', q + EPS, jnp.cumsum(k, axis=2) + EPS)
            src_out = normal / jnp.einsum('bhld,bhld->bhl', k + EPS, jnp.cumsum(q, axis=2) + EPS)
            cons_sink = jnp.einsum('bhld,bhld->bhl', q + EPS, jnp.cumsum(k * src_out[..., None], axis=2) + EPS) / normal
            cons_src = jnp.einsum('bhld,bhld->bhl', k + EPS, jnp.cumsum(q * sink_in[..., None], axis=2) + EPS) / normal
            cons_src = jnp.clip(cons_src, -1.0, 1.0)
            sink_alloc = jax.nn.sigmoid(cons_sink)
            cons_src = jnp.exp(cons_src)
            src_comp = cons_src / jnp.cumsum(cons_src, axis=-1) * normal
            qs = q * (sink_in / normal)[..., None]
            vs = v * src_comp[..., None]
            kv = jnp.cumsum(jnp.einsum('bhld,bhlm->bhldm', k, vs), axis=2)
            x = jnp.einsum('bhld,bhldm->bhlm', qs, kv) * sink_alloc[..., None]
            x = x.transpose(0, 2, 1, 3).reshape(Bn, Ln, Dn)
            attn = x @ Wo + bo
            h = _layernorm(inputs + attn, ln1_g, ln1_b)
            ffn = jax.nn.gelu(h @ W1 + b1, approximate=False) @ W2 + b2
            return _layernorm(h + ffn, ln2_g, ln2_b)
        key = jax.random.key(seed)
        ks = jax.random.split(key, 12)

        def w(k, shape):
            return jax.random.normal(k, shape, dtype=jnp.float32) * 0.02
        return {'inputs': jax.random.normal(ks[0], (B, L, D), dtype=jnp.float32), 'attn_mask': jnp.zeros((L, L), dtype=jnp.bool_), 'Wq': w(ks[1], (D, D)), 'bq': jnp.zeros((D,), jnp.float32), 'Wk': w(ks[2], (D, D)), 'bk': jnp.zeros((D,), jnp.float32), 'Wv': w(ks[3], (D, D)), 'bv': jnp.zeros((D,), jnp.float32), 'Wo': w(ks[4], (D, D)), 'bo': jnp.zeros((D,), jnp.float32), 'ln1_g': jnp.ones((D,), jnp.float32), 'ln1_b': jnp.zeros((D,), jnp.float32), 'W1': w(ks[5], (D, F)), 'b1': jnp.zeros((F,), jnp.float32), 'W2': w(ks[6], (F, D)), 'b2': jnp.zeros((D,), jnp.float32), 'ln2_g': jnp.ones((D,), jnp.float32), 'ln2_b': jnp.zeros((D,), jnp.float32)}
    _L0_attn_in = _L0_attn_setup()

    def _L0_ffn_setup():
        import jax, jax.numpy as jnp
        import numpy as np
        B, T, D, E = (4, 256, 256, 8)
        HD = 4 * D
        key = jax.random.key(seed)
        k1, k2, k3, k4 = jax.random.split(key, 4)
        std = 0.5 * D ** (-0.5)
        bound = 3.0 ** 0.5 * std
        x = jax.random.normal(k1, (B, T, D), dtype=jnp.float32)
        router_w = jax.random.normal(k2, (E, D), dtype=jnp.float32) * 0.02
        expert_fc = jax.random.uniform(k3, (E, D, HD), dtype=jnp.float32, minval=-bound, maxval=bound)
        expert_proj = jax.random.normal(k4, (E, D, HD), dtype=jnp.float32) * 0.02
        return {'x': x, 'router_w': router_w, 'expert_fc': expert_fc, 'expert_proj': expert_proj}
    _L0_ffn_in = _L0_ffn_setup()
    _d = {'L0_attn_inputs': _L0_attn_in['inputs'], 'L0_attn_attn_mask': _L0_attn_in['attn_mask'], 'L0_attn_Wq': _L0_attn_in['Wq'], 'L0_attn_bq': _L0_attn_in['bq'], 'L0_attn_Wk': _L0_attn_in['Wk'], 'L0_attn_bk': _L0_attn_in['bk'], 'L0_attn_Wv': _L0_attn_in['Wv'], 'L0_attn_bv': _L0_attn_in['bv'], 'L0_attn_Wo': _L0_attn_in['Wo'], 'L0_attn_bo': _L0_attn_in['bo'], 'L0_attn_ln1_g': _L0_attn_in['ln1_g'], 'L0_attn_ln1_b': _L0_attn_in['ln1_b'], 'L0_attn_W1': _L0_attn_in['W1'], 'L0_attn_b1': _L0_attn_in['b1'], 'L0_attn_W2': _L0_attn_in['W2'], 'L0_attn_b2': _L0_attn_in['b2'], 'L0_attn_ln2_g': _L0_attn_in['ln2_g'], 'L0_attn_ln2_b': _L0_attn_in['ln2_b'], 'L0_ffn_router_w': _L0_ffn_in['router_w'], 'L0_ffn_expert_fc': _L0_ffn_in['expert_fc'], 'L0_ffn_expert_proj': _L0_ffn_in['expert_proj']}
    _x0 = _d['L0_attn_inputs']
    _d['L0_attn_inputs'] = jax.random.normal(jax.random.fold_in(jax.random.key(seed), 1), (4, 1024, 256), dtype=_x0.dtype)
    del _x0
    return _d

def reference(L0_attn_inputs, L0_attn_attn_mask, L0_attn_Wq, L0_attn_bq, L0_attn_Wk, L0_attn_bk, L0_attn_Wv, L0_attn_bv, L0_attn_Wo, L0_attn_bo, L0_attn_ln1_g, L0_attn_ln1_b, L0_attn_W1, L0_attn_b1, L0_attn_W2, L0_attn_b2, L0_attn_ln2_g, L0_attn_ln2_b, L0_ffn_router_w, L0_ffn_expert_fc, L0_ffn_expert_proj):

    def _L0_attn_ref(inputs, attn_mask, Wq, bq, Wk, bk, Wv, bv, Wo, bo, ln1_g, ln1_b, W1, b1, W2, b2, ln2_g, ln2_b):
        import jax, jax.numpy as jnp
        import numpy as np
        B, L, D, H, F = (2, 256, 256, 16, 1024)
        DH = D // H
        EPS = 1e-06

        def _layernorm(x, g, b, eps=1e-05):
            m = jnp.mean(x, axis=-1, keepdims=True)
            v = jnp.mean((x - m) ** 2, axis=-1, keepdims=True)
            return (x - m) / jnp.sqrt(v + eps) * g + b

        def _decoder_layer(inputs, Wq, bq, Wk, bk, Wv, bv, Wo, bo, ln1_g, ln1_b, W1, b1, W2, b2, ln2_g, ln2_b):
            Bn, Ln, Dn = inputs.shape

            def heads(W, b):
                return (inputs @ W + b).reshape(Bn, Ln, H, DH).transpose(0, 2, 1, 3)
            q = jax.nn.sigmoid(heads(Wq, bq))
            k = jax.nn.sigmoid(heads(Wk, bk))
            v = heads(Wv, bv)
            normal = (jnp.arange(Ln, dtype=jnp.float32) + 1.0)[None, None, :]
            sink_in = normal / jnp.einsum('bhld,bhld->bhl', q + EPS, jnp.cumsum(k, axis=2) + EPS)
            src_out = normal / jnp.einsum('bhld,bhld->bhl', k + EPS, jnp.cumsum(q, axis=2) + EPS)
            cons_sink = jnp.einsum('bhld,bhld->bhl', q + EPS, jnp.cumsum(k * src_out[..., None], axis=2) + EPS) / normal
            cons_src = jnp.einsum('bhld,bhld->bhl', k + EPS, jnp.cumsum(q * sink_in[..., None], axis=2) + EPS) / normal
            cons_src = jnp.clip(cons_src, -1.0, 1.0)
            sink_alloc = jax.nn.sigmoid(cons_sink)
            cons_src = jnp.exp(cons_src)
            src_comp = cons_src / jnp.cumsum(cons_src, axis=-1) * normal
            qs = q * (sink_in / normal)[..., None]
            vs = v * src_comp[..., None]
            kv = jnp.cumsum(jnp.einsum('bhld,bhlm->bhldm', k, vs), axis=2)
            x = jnp.einsum('bhld,bhldm->bhlm', qs, kv) * sink_alloc[..., None]
            x = x.transpose(0, 2, 1, 3).reshape(Bn, Ln, Dn)
            attn = x @ Wo + bo
            h = _layernorm(inputs + attn, ln1_g, ln1_b)
            ffn = jax.nn.gelu(h @ W1 + b1, approximate=False) @ W2 + b2
            return _layernorm(h + ffn, ln2_g, ln2_b)
        return _decoder_layer(inputs, Wq, bq, Wk, bk, Wv, bv, Wo, bo, ln1_g, ln1_b, W1, b1, W2, b2, ln2_g, ln2_b)

    def _L0_ffn_ref(x, router_w, expert_fc, expert_proj):
        import jax, jax.numpy as jnp
        import numpy as np
        B, T, D, E = (4, 256, 256, 8)
        HD = 4 * D
        logits = jnp.einsum('btd,ed->bte', x, router_w)
        probs = jax.nn.softmax(logits, axis=-1)
        expert_ids = jnp.argmax(probs, axis=-1)
        mask = jax.nn.one_hot(expert_ids, E, dtype=x.dtype)
        h = jnp.einsum('btd,edh->ebth', x, expert_fc)
        h = jnp.square(jax.nn.relu(h))
        out_e = jnp.einsum('ebth,edh->ebtd', h, expert_proj)
        output = jnp.einsum('ebtd,bte->btd', out_e, mask)
        return output
    x = L0_attn_inputs
    x = _layernorm(x + _L0_attn_ref(x, L0_attn_attn_mask, L0_attn_Wq, L0_attn_bq, L0_attn_Wk, L0_attn_bk, L0_attn_Wv, L0_attn_bv, L0_attn_Wo, L0_attn_bo, L0_attn_ln1_g, L0_attn_ln1_b, L0_attn_W1, L0_attn_b1, L0_attn_W2, L0_attn_b2, L0_attn_ln2_g, L0_attn_ln2_b), axis=-1)
    x = _layernorm(x + _L0_ffn_ref(x, L0_ffn_router_w, L0_ffn_expert_fc, L0_ffn_expert_proj), axis=-1)
    return x

_drawn_inputs = setup_inputs


def setup_inputs(seed=0):
    import zlib

    import numpy as np

    out = dict(_drawn_inputs(seed))
    spreads = {'L0_attn_bq': (0.0, 0.8),
     'L0_attn_bk': (0.0, 0.8),
     'L0_attn_bv': (0.0, 0.1),
     'L0_attn_bo': (0.0, 0.1),
     'L0_attn_ln1_g': (1.0, 0.2),
     'L0_attn_ln1_b': (0.0, 0.1),
     'L0_attn_b1': (0.0, 0.1),
     'L0_attn_b2': (0.0, 0.1),
     'L0_attn_ln2_g': (1.0, 0.2),
     'L0_attn_ln2_b': (0.0, 0.1)}
    factors = {'L0_attn_Wq': 8.0, 'L0_attn_Wk': 8.0, 'L0_attn_Wv': 5.929}
    for name, (base, spread) in spreads.items():
        noise = np.random.default_rng([zlib.crc32(name.encode()), seed]).standard_normal(out[name].shape)
        drawn = base * np.exp(spread * noise) if base else spread * noise
        out[name] = jnp.asarray(drawn.astype(out[name].dtype))
    for name, factor in factors.items():
        out[name] = (out[name] * factor).astype(out[name].dtype)
    return out
```

```python
from contextlib import ExitStack

import concourse.bass as bass
from concourse import mybir

ALU = mybir.AluOpType
ACT = mybir.ActivationFunctionType
F32 = mybir.dt.float32
I32 = mybir.dt.int32
AX_X = mybir.AxisListType.X

P = 128
B, L, D = 4, 1024, 256
TOK = B * L
H, DH = 16, 16
F = 1024
E, HD = 8, 1024
EPS_FLOW, EPS_LN = 1e-6, 1e-5

KT = D // P
T = 512
NC = T // P
G = TOK // T
GPB = L // T
NT = TOK // P
FT = F // P
HPT = P // DH
ROW = D + 4
SLOTS = NT + E - 1
FE = HD // P
UNDER_FFN = 3
NO_TOKEN = 1 << 20


class Event:

    def __init__(self, sem, per):
        self.sem, self.per = sem, per

    def wait(self, eng, g, k):
        value = g * self.per + k
        if not isinstance(value, int) or value > 0:
            eng.wait_ge(self.sem, value)


EVENTS = {
    "proj": 6, "sig": 4, "v": 2, "scan1": 4, "carry1": 1, "dot1": 2, "hs1": 1, "rden": 1, "cz": 1,
    "czt": 1, "cztc": 1, "bc1": 4, "scaled": 4, "scan2": 4, "carry2": 1, "dot2": 2, "hs2": 1, "cons": 1,
    "clip": 1, "exps": 2, "cum": 1, "csum": 1, "carry3": 1, "csr": 1, "comp0": 1, "comp": 1, "al0": 1,
    "al1": 1, "s3": 1, "s3t": 1, "s3tc": 1, "vp": NC, "bc3": 2, "qp": 2,
    "qm0": NC, "qm1": NC, "kt": NC, "ktc": NC, "s": 4 * NC, "sm": 4 * NC, "av": NC, "upd": NC, "sttmp": NC,
    "st": NC, "xatc": NC, "wo": NC, "xb": 1, "r1": NC, "bs1": NC, "ba1": NC, "ve1": NC, "rs1": NC, "n1": NC,
    "hg": NC, "h1": NC, "h1b": NC,
    "h1t": 2, "h1tc": 2, "w1": FT, "gelu": FT, "w2": FT, "r2": NC, "bs2": NC, "ba2": NC, "ve2": NC, "rs2": NC,
    "n2": NC, "lg2": NC, "l2": NC, "r3": NC, "bs3": NC, "ba3": NC, "ve3": NC, "rs3": NC, "xn": NC, "xr": NC,
    "xrt": NC, "xrtc": NC, "lgm": NC, "lg": NC,
}

SCHEDULE = [
    ("a_proj", 0), ("b_turn", 0), ("b_ffn", 0), ("a_dots1", 0), ("b_ffn", 1), ("a_share1", 0), ("b_ffn", 2),
    ("b_ffn", 3), ("a_dots2", 0), ("b_ffn", 4), ("a_comp", 0), ("a_share2", 0), ("b_ffn", 5), ("a_pairs", 0),
    ("b_ffn", 6), ("a_mix", 0), ("b_ffn", 7), ("a_pairs", 1), ("b_ffn", 8), ("b_tail", 0), ("a_mix", 1),
    ("b_tail", 1), ("a_pairs", 2), ("b_route", 0), ("b_tail", 2), ("a_mix", 2), ("b_logit", 0), ("b_route", 1),
    ("b_tail", 3), ("a_pairs", 3), ("b_logit", 1), ("b_route", 2), ("b_tail", 4), ("a_mix", 3), ("b_logit", 2),
    ("b_route", 3), ("b_logit", 3),
]


def all_groups(eng, steps):
    def beside(ga, half, gb):
        for name, i in SCHEDULE:
            if name in steps:
                if name[0] == "a" and ga is not None:
                    steps[name](ga, half, i)
                if name[0] == "b" and gb is not None:
                    steps[name](gb, 1 - half, i)

    beside(0, 0, None)
    beside(1, 1, 0)
    with eng.Fori(1, G // 2) as i:
        beside(i * 2, 0, i * 2 - 1)
        beside(i * 2 + 1, 1, i * 2)
    beside(None, 0, G - 1)


def build(nc, x_d, xT_d, wqkvo_d, bq_d, bk_d, bv_d, bo_d, g1_d, be1_d, w1_d, b1_d, w2_d, b2_d, g2_d, be2_d,
          rw_d, fc_d, pj_d, out_d):
    ctx = ExitStack()
    with ctx:
        def sb(name, shape, dt=F32, stack=ctx):
            return stack.enter_context(nc.sbuf_tensor(name, shape, dt))

        def sem(name):
            return ctx.enter_context(nc.semaphore(name))

        ident = sb("ident", [P, P])
        upto = sb("upto", [P, P])
        before = sb("before", [P, P])
        ones = sb("ones", [P, P])
        xr = sb("xr", [P, NT, ROW])
        logits = sb("logits", [P, NT, E])
        minus_half = sb("minus_half", [P, 1])
        early, early_i = sb("early", [P, E]), sb("early_i", [P, E], I32)
        tile_at, tile_at_i = sb("tile_at", [P, SLOTS]), sb("tile_at_i", [P, SLOTS], I32)


        part1 = ExitStack()

        def s1(name, shape, dt=F32):
            return sb(name, shape, dt, part1)

        w1 = s1("w1s", [P, KT, F])
        w2 = s1("w2s", [P, FT, D])
        rw = s1("rw", [P, KT, E])
        b1 = s1("b1s", [P, FT])
        b2, g2, be2 = s1("b2s", [P, D]), s1("g2s", [P, D]), s1("be2s", [P, D])
        x = s1("x", [P, 2, NC, D])
        h1 = s1("h1", [P, 2, NC, D])
        h1b = s1("h1b", [P, 2, NC, D])
        h1T = s1("h1T", [P, KT, T])
        hT = s1("hT", [P, 2, T])
        r2, n2, lg2, l2, r3, xn = (s1(n, [P, 2, D]) for n in ("r2", "n2", "lg2", "l2", "r3", "xn"))
        bst = s1("bst", [P, 3, 2, 6])
        mv = s1("mv", [P, 3, 2, 2])
        vare, rstd = s1("vare", [P, 3, 2, 1]), s1("rstd", [P, 3, 2, 1])
        xrT = s1("xrT", [P, KT, P])
        empty = s1("empty", [P, ROW])
        wqkvo = s1("wqkvo", [P, 4, KT, D])
        bq, bk = s1("bqs", [P, KT]), s1("bks", [P, KT])
        bv, bo, g1, be1 = (s1(n, [P, D]) for n in ("bvs", "bos", "g1s", "be1s"))
        head_of = s1("head_of", [P, HPT])
        same_head = s1("same_head", [P, P])
        share = s1("share", [P, 2 * NC, KT, P])
        ones_t = s1("ones_t", [P, T])
        normal, normal_i = s1("normal", [P, L // P]), s1("normal_i", [P, L // P], I32)
        rnormal = s1("rnormal", [P, L // P])
        xT = s1("xT", [P, 2, KT, T])
        qT = s1("qT", [P, KT, T])
        kT = s1("kT", [P, KT, T])
        cc = s1("cc", [P, 2, KT, T])
        carry1, carry2 = s1("carry1", [P, 2 * KT]), s1("carry2", [P, 2 * KT])
        carry3 = s1("carry3", [P, H])
        rden = s1("rden", [P, 2, NC, H])
        cz, cz2 = s1("cz", [P, 2, NC, H]), s1("cz2", [P, 2, NC, H])
        czT, s3T = s1("czT", [P, P]), s1("s3T", [P, P])
        cons = s1("cons", [P, 2, NC, H])
        ex = s1("ex", [P, 2, NC, H])
        csum, csr, comp0 = (s1(n, [P, NC, H]) for n in ("csum", "csr", "comp0"))
        al0, al1 = s1("al0", [P, NC, H]), s1("al1", [P, NC, H])
        v = s1("v", [P, NC, D])
        vpad = s1("vpad", [P, NC, H // 2, 6 * DH])
        qm = s1("qm", [P, KT, HPT, P])
        sm = s1("sm", [P, 4, 4, P])
        ktok = s1("ktok", [P, 2, D])
        state, sttmp = s1("state", [P, KT, P]), s1("sttmp", [P, KT, P])
        xat = s1("xat", [P, 2, KT, P])
        xb = s1("xb", [P, NC, D])
        r1, n1, hg = s1("r1", [P, 2, D]), s1("n1", [P, 2, D]), s1("hg", [P, 2, D])
        part1.close()

        part2 = ExitStack()

        def s2(name, shape, dt=F32):
            return sb(name, shape, dt, part2)

        xs = s2("xs", [P, 3, ROW])
        xsT = s2("xsT", [P, KT, P])
        relu = s2("relu", [P, HD])
        actT = s2("actT", [P, FE, P])
        res, y = s2("res", [P, 3, D]), s2("y", [P, 3, D])
        mst, mmv = s2("mst", [P, 3, 6]), s2("mmv", [P, 3, 2])
        mvare, mrstd = s2("mvare", [P, 3, 1]), s2("mrstd", [P, 3, 1])
        best, first = s2("best", [P, NT]), s2("first", [P, NT])
        hit, key, onehot = (s2(n, [P, NT, E]) for n in ("hit", "key", "onehot"))
        total, upto_tile = s2("total", [P, NT, E]), s2("upto_tile", [P, NT, E])
        count_i, filled = s2("count_i", [P, E], I32), s2("filled", [P, E])
        end, begin_at = s2("end", [P, E]), s2("begin_at", [P, E])
        place = s2("place", [P, NT, E])
        place_own, slot_f = s2("place_own", [P, NT, E]), s2("slot_f", [P, NT])
        slot = s2("slot", [P, NT], I32)
        passed, expert_f = s2("passed", [P, SLOTS, E]), s2("expert_f", [P, SLOTS])
        expert = s2("expert", [P, SLOTS], I32)
        we = s2("we", [P, E, 2, KT * HD])
        part2.close()

        bank = [ctx.enter_context(nc.psum_tensor(f"bank{n}", [P, 512], F32)) for n in range(8)]
        pa, ps0, ps1, pm, pc, pb, po0, po1 = bank
        SUMS, TURN, UPTO, TOTAL, ROUTE = 0, 128, 256, 320, 352
        BANK4 = [pa, ps0, ps1, pm]

        xs_d = nc.dram_tensor("routed_rows", [SLOTS * P, ROW], F32, kind="Internal").ap()

        ev = {name: Event(sem(name), per) for name, per in EVENTS.items()}
        S = {name: ev[name].sem for name in ev}
        weights_in, tables_in = sem("weights_in"), sem("tables_in")
        xT_in, x_in = [sem("xT_in0"), sem("xT_in1")], [sem("x_in0"), sem("x_in1")]
        masks, masks_done = sem("masks"), sem("masks_done")
        vector_ready = sem("vector_ready")
        apart_sem = sem("waits_apart")
        cleared = sem("cleared")
        experts_in = [sem(f"expert{e}_in") for e in range(E)]
        scattered, gone = sem("scattered"), sem("gone")
        rt = sem("routing_step")
        sums_up = sem("sums_up")
        xs_in = [sem(f"xs_in{n}") for n in range(3)]
        y_out = [sem(f"y_out{n}") for n in range(3)]
        M = {name: Event(sem("m_" + name), per) for name, per in {
            "turned": 1, "xsT": 1, "up": 2, "relu0": 1, "relu1": 1, "hturned": 2, "act": 2, "down": 1,
            "res": 1, "stats": 1, "aggr": 1, "vare": 1, "rstd": 1, "y": 1}.items()}

        block = ctx.enter_context(nc.Block())

        def apart(eng):
            eng.sem_inc(apart_sem, 1)

        def chunk(c):
            return slice(c * P, (c + 1) * P)

        def row(g, c):
            if isinstance(g, int):
                return xr[:, g * NC + c, 0:D]
            return xr[:, bass.ds(g * NC + c, 1), 0:D].rearrange("p a d -> p (a d)")

        def diag(c):
            return vpad[:, c].rearrange("p j (e k) -> p j e k", e=2)[:, :, :, 0:DH]

        fc = we[:, :, 0, :].rearrange("p e (k n) -> p e k n", k=KT)
        pj = we[:, :, 1, :].rearrange("p e (k n) -> p e k n", k=FE)

        def spread_q(eng, m, g, c):
            ev["qp"].wait(eng, g, m + 1)
            ev["s"].wait(eng, g, 4 * c - 2 + 2 * m)
            eng.tensor_tensor(qm[:, m], cc[:, 0, m, chunk(c)].unsqueeze(1).broadcast_to([P, HPT, P]),
                              head_of[:].unsqueeze(2).broadcast_to([P, HPT, P]), ALU.mult)\
                .then_inc(S[f"qm{m}"], 1)

        @block.sync
        def _(sp):
            sp.dma_start(wqkvo[:], wqkvo_d.rearrange("w (k p) n -> p w k n", p=P)).then_inc(weights_in, 16)
            for tile, src in ((bq, bq_d), (bk, bk_d), (b1, b1_d)):
                sp.dma_start(tile[:], src).then_inc(weights_in, 16)

            def load_xT(g, half):
                if not isinstance(g, int):
                    ev["proj"].wait(sp, g - 2, 6)
                sp.dma_start(xT[:, half], xT_d[:, :, g * T:g * T + T] if isinstance(g, int) else
                             xT_d[:, :, bass.ds(g * T, T)]).then_inc(xT_in[half], 16)

            def load_x(g, half):
                if not isinstance(g, int):
                    ev["r3"].wait(sp, g - 2, NC)
                src = x_d[:, g * NC:g * NC + NC] if isinstance(g, int) else x_d[:, bass.ds(g * NC, NC)]
                sp.dma_start(x[:, half], src).then_inc(x_in[half], 16)

            load_xT(0, 0)
            for tile, src in ((bv, bv_d), (bo, bo_d), (g1, g1_d), (be1, be1_d), (b2, b2_d), (g2, g2_d),
                              (be2, be2_d)):
                sp.dma_start(tile[:], src.rearrange("(a n) -> a n", a=1).broadcast_to([P, D]))\
                    .then_inc(tables_in, 16)
            load_x(0, 0)
            sp.dma_start(w1[:], w1_d.rearrange("(k p) n -> p k n", p=P)).then_inc(tables_in, 16)
            sp.dma_start(w2[:], w2_d.rearrange("(k p) n -> p k n", p=P)).then_inc(tables_in, 16)
            sp.dma_start(rw[:], rw_d.rearrange("(k p) n -> p k n", p=P)).then_inc(tables_in, 16)
            load_xT(1, 1)
            load_x(1, 1)
            sp.wait_ge(cleared, 1)
            for a in range(3):
                n = SLOTS // 3
                sp.dma_start(xs_d.rearrange("(s p) r -> p s r", p=P)[:, a * n:a * n + n, :],
                             empty[:].unsqueeze(1).broadcast_to([P, n, ROW])).then_inc(gone, 16)
            with sp.Fori(1, G // 2) as i:
                for half in range(2):
                    load_xT(i * 2 + half, half)
                    load_x(i * 2 + half, half)
            def load_expert(e):
                sp.dma_start(fc[:, e], fc_d[e].rearrange("(k p) n -> p k n", p=P)).then_inc(experts_in[e], 16)
                sp.dma_start(pj[:, e], pj_d[e].rearrange("(k p) n -> p k n", p=P)).then_inc(experts_in[e], 16)

            ev["h1"].wait(sp, G - 1, NC)
            for e in range(UNDER_FFN, E):
                load_expert(e)
            for name in ("h1b", "l2", "xr", "lg"):
                ev[name].wait(sp, G - 1, NC)
            for e in range(UNDER_FFN):
                load_expert(e)
            sp.wait_ge(scattered, 16 * NT)

            def load_rows(t, s):
                j = t * 3 + s
                if not isinstance(t, int):
                    M["res"].wait(sp, j - 3, 1)
                    apart(sp)
                    sp.wait_ge(y_out[s], t * 16)
                    apart(sp)
                src = xs_d[j * P:j * P + P, :] if isinstance(j, int) else xs_d[bass.ds(j * P, P), :]
                sp.dma_start(xs[:, s], src).then_inc(xs_in[s], 16)

            for s in range(3):
                load_rows(0, s)
            with sp.Fori(1, SLOTS // 3) as t:
                for s in range(3):
                    load_rows(t, s)
            for s in range(3):
                sp.wait_ge(y_out[s], SLOTS // 3 * 16)

        @block.tensor
        def _(pe):
            pe.wait_ge(weights_in, 16 * 4)
            pe.wait_ge(masks_done, 1)
            wq, wk, wv, wo = (wqkvo[:, n] for n in range(4))

            def project(g, half, _):
                pe.wait_ge(xT_in[half], (g - half) * 8 + 16)
                for n, w in enumerate((wq, wq, wk, wk)):
                    m = n % 2
                    if n == 0:
                        ev["r1"].wait(pe, g - 1, NC)
                    if n == 1:
                        ev["sttmp"].wait(pe, g - 1, NC)
                    if n == 2:
                        ev["sm"].wait(pe, g - 1, 4 * NC)
                    if n == 3:
                        ev["xatc"].wait(pe, g - 1, NC)
                    for k in range(KT):
                        last = nc.tensor.matmul(BANK4[n][:], w[:, k, chunk(m)], xT[:, half, k, :],
                                                start=(k == 0), stop=(k == KT - 1))
                    last.then_inc(S["proj"], 1)
                for n in range(2):
                    ev["sig"].wait(pe, g, n + 1)
                    for c in range(2):
                        for k in range(KT):
                            last = nc.tensor.matmul(BANK4[n][:, c * D:c * D + D], xT[:, half, k, chunk(2 * n + c)],
                                                    wv[:, k, :], start=(k == 0), stop=(k == KT - 1))
                    last.then_inc(S["proj"], 1)

            def dots(g, ready, done):
                ev[ready].wait(pe, g, 2)
                for w in range(2):
                    for c in range(NC):
                        for m in range(KT):
                            at = SUMS + (w * NC + c) * H + m * HPT
                            last = nc.tensor.matmul(pc[:, at:at + HPT], cc[:, w, m, chunk(c)], head_of[:],
                                                    start=True, stop=True)
                last.then_inc(S[done], 1)

            def dots1(g, half, _):
                dots(g, "dot1", "hs1")
                ev["cz"].wait(pe, g, 1)
                nc.tensor.transpose(pc[:, TURN:TURN + P], cz[:].rearrange("p w c h -> p (w c h)"), ident[:])\
                    .then_inc(S["czt"], 1)

            def share1(g, half, _):
                ev["cztc"].wait(pe, g, 1)
                for n in range(4):
                    w, m = n // 2, n % 2
                    if n < 2:
                        ev["v"].wait(pe, g, n + 1)
                    else:
                        ev["sig"].wait(pe, g, n + 1)
                    for c in range(NC):
                        last = nc.tensor.matmul(BANK4[n][:, chunk(c)], share[:, w * NC + c, m, :], czT[:],
                                                start=True, stop=True)
                    last.then_inc(S["bc1"], 1)

            def dots2(g, half, _):
                dots(g, "dot2", "hs2")

            def comp(g, half, _):
                ev["exps"].wait(pe, g, 2)
                for c in range(NC):
                    nc.tensor.matmul(pc[:, UPTO + c * H:UPTO + (c + 1) * H], upto[:], ex[:, 1, c, :],
                                     start=(c == 0), stop=(c == 0), skip_group_check=True)
                    for later in range(c + 1, NC):
                        nc.tensor.matmul(pc[:, UPTO + later * H:UPTO + (later + 1) * H], ones[:], ex[:, 1, c, :],
                                         start=False, stop=False, skip_group_check=True)
                for c in range(NC):
                    last = nc.tensor.matmul(pc[:, TOTAL:TOTAL + H], ones[:], ex[:, 1, c, :],
                                            start=(c == 0), stop=(c == NC - 1))
                last.then_inc(S["cum"], 1)
                ev["s3"].wait(pe, g, 1)
                nc.tensor.transpose(pc[:, TURN:TURN + P], cz2[:].rearrange("p w c h -> p (w c h)"), ident[:])\
                    .then_inc(S["s3t"], 1)

            def share2(g, half, _):
                ev["s3tc"].wait(pe, g, 1)
                for m in range(KT):
                    ev["scaled"].wait(pe, g, m + 1)
                    for c in range(NC):
                        last = nc.tensor.matmul(BANK4[m][:, chunk(c)], share[:, c, m, :], s3T[:],
                                                start=True, stop=True)
                    last.then_inc(S["bc3"], 1)

            def pairs(g, half, c):
                if c == 0:
                    ev["scaled"].wait(pe, g, 4)
                else:
                    ev["xatc"].wait(pe, g, c)
                for m in range(KT):
                    last = nc.tensor.transpose(pm[:, chunk(m)], kT[:, m, chunk(c)], ident[:])
                last.then_inc(S["kt"], 1)
                for m in range(KT):
                    ev[f"qm{m}"].wait(pe, g, c + 1)
                    for i, dst in enumerate((ps0, ps1)):
                        if c == 0 and m == 0 and i == 0:
                            ev["qp"].wait(pe, g, 2)
                        elif m == 0 and i == 0:
                            ev["sttmp"].wait(pe, g, c)
                        else:
                            ev["sm"].wait(pe, g, 4 * c + 2 * m + i - 1)
                        nc.tensor.matmul(dst[:], kT[:, m, chunk(c)],
                                         qm[:, m, 4 * i:4 * i + 4, :].rearrange("p h t -> p (h t)"),
                                         start=True, stop=True).then_inc(S["s"], 1)

            def mix(g, half, c):
                fresh = half == 0 and c == 0
                ev["ktc"].wait(pe, g, c + 1)
                if not fresh:
                    ev["st"].wait(pe, g, c)
                    for m in range(KT):
                        nc.tensor.matmul(pm[:, chunk(m)], state[:, m, :], cc[:, 0, m, chunk(c)],
                                         start=(m == 0), stop=False, skip_group_check=True)
                ev["vp"].wait(pe, g, c + 1)
                for m in range(KT):
                    for j in range(HPT // 2):
                        if j % 2 == 0:
                            ev["sm"].wait(pe, g, 4 * c + 2 * m + j // 2 + 1)
                        for e in range(2):
                            last = nc.tensor.matmul(
                                pm[32 * j:32 * j + 32, chunk(m)], vpad[:, c, 4 * m + j, 32 * e:32 * e + 32],
                                sm[:, 2 * m + j // 2, 2 * (j % 2) + e, :],
                                start=(fresh and m == 0 and e == 0), stop=False, skip_group_check=True)
                last.then_inc(S["av"], 1)
                for m in range(KT):
                    last = nc.tensor.matmul(ps0[:, chunk(m)], ktok[:, c % 2, chunk(m)],
                                            diag(c)[:, 4 * m:4 * m + 4], start=True, stop=True,
                                            skip_group_check=True)
                last.then_inc(S["upd"], 1)
                ev["xatc"].wait(pe, g, c + 1)
                if c == 0:
                    ev["qp"].wait(pe, g, 1)
                else:
                    ev["r1"].wait(pe, g, c)
                for m in range(KT):
                    last = nc.tensor.matmul(pa[:, 0:D], xat[:, c % 2, m, :], wo[:, m, :],
                                            start=(m == 0), stop=(m == KT - 1))
                last.then_inc(S["wo"], 1)

            def turn(g, half, _):
                ev["h1"].wait(pe, g, NC)
                for m in range(KT):
                    if m == 0:
                        ev["xrtc"].wait(pe, g - 1, NC)
                    else:
                        ev["h1tc"].wait(pe, g, 1)
                    for c in range(NC):
                        last = nc.tensor.transpose(pb[:, chunk(c)], h1[:, half, c, chunk(m)], ident[:])
                    last.then_inc(S["h1t"], 1)

            def ffn(g, half, f):
                if f < FT:
                    if f == 0:
                        ev["h1tc"].wait(pe, g, 2)
                    else:
                        ev["gelu"].wait(pe, g, f)
                    for k in range(KT):
                        last = nc.tensor.matmul(pb[:], w1[:, k, chunk(f)], h1T[:, k, :], start=(k == 0),
                                                stop=(k == KT - 1))
                    last.then_inc(S["w1"], 1)
                if f > 0:
                    ev["gelu"].wait(pe, g, f)
                    if f == 1:
                        ev["r2"].wait(pe, g - 1, NC)
                    for c in range(NC):
                        last = nc.tensor.matmul((po0, po1)[c // 2][:, (c % 2) * D:(c % 2) * D + D],
                                                hT[:, (f - 1) % 2, chunk(c)], w2[:, f - 1, :],
                                                start=(f == 1 and c % 2 == 0), stop=(f == FT),
                                                skip_group_check=True)
                    last.then_inc(S["w2"], 1)

            def route(g, half, c):
                ev["xn"].wait(pe, g, c + 1)
                if c == 0:
                    ev["gelu"].wait(pe, g, FT)
                ev["xrtc"].wait(pe, g, c)
                for m in range(KT):
                    last = nc.tensor.transpose(pb[:, chunk(m)], xn[:, c % 2, chunk(m)], ident[:])
                last.then_inc(S["xrt"], 1)

            def logit(g, half, c):
                ev["xrtc"].wait(pe, g, c + 1)
                ev["lg"].wait(pe, g, c)
                for m in range(KT):
                    last = nc.tensor.matmul(pc[:, ROUTE:ROUTE + E], xrT[:, m, :],
                                            rw[:, m, :], start=(m == 0), stop=(m == KT - 1))
                last.then_inc(S["lgm"], 1)

            pe.wait_ge(tables_in, 16 * 10)
            all_groups(pe, {"a_proj": project, "a_dots1": dots1, "a_share1": share1, "a_dots2": dots2,
                            "a_comp": comp, "a_share2": share2, "a_pairs": pairs, "a_mix": mix,
                            "b_turn": turn, "b_ffn": ffn, "b_route": route, "b_logit": logit})

            pe.wait_ge(rt, R_ONEHOT)
            flat = onehot[:].rearrange("p t e -> p (t e)")
            nc.tensor.matmul(pa[:, 0:NT * E], before[:], flat, start=True, stop=True)
            nc.tensor.matmul(ps0[:, 0:NT * E], ones[:], flat, start=True, stop=True).then_inc(sums_up, 1)

            h_bank, ht_bank, x_bank, o_bank = (ps0, ps1), (pm, pc), pa, pb

            def turn_rows(t, s):
                j = t * 3 + s
                pe.wait_ge(xs_in[s], t * 16 + 16)
                M["xsT"].wait(pe, j - 1, 1)
                for m in range(KT):
                    last = nc.tensor.transpose(x_bank[:, chunk(m)], xs[:, s, chunk(m)], ident[:])
                last.then_inc(M["turned"].sem, 1)

            def expert_of(j):
                at = expert[0:1, j:j + 1] if isinstance(j, int) else expert[0:1, bass.ds(j, 1)]
                return pe.value_load(at, min_val=0, max_val=E - 1)

            def up(j, e):
                M["xsT"].wait(pe, j, 1)
                for n in range(2):
                    M[f"relu{n}"].wait(pe, j - 1, 1)
                    for k in range(KT):
                        last = nc.tensor.matmul(h_bank[n][:], xsT[:, k, :], fc[:, bass.ds(e, 1), k, n * 512:n * 512 + 512].rearrange("p a n -> p (a n)"),
                                                start=(k == 0), stop=(k == KT - 1))
                    last.then_inc(M["up"].sem, 1)

            def down(j, e):
                M["act"].wait(pe, j, 2)
                M["res"].wait(pe, j - 1, 1)
                for f in range(FE):
                    last = nc.tensor.matmul(o_bank[:, 0:D], actT[:, f, :], pj[:, bass.ds(e, 1), f, :].rearrange("p a n -> p (a n)"),
                                            start=(f == 0), stop=(f == FE - 1))
                last.then_inc(M["down"].sem, 1)

            def turn_hidden(j):
                for n in range(2):
                    M[f"relu{n}"].wait(pe, j, 1)
                    M["act"].wait(pe, j - 1, n + 1)
                    for f in range(4):
                        last = nc.tensor.transpose(ht_bank[n][:, chunk(f)], relu[:, chunk(4 * n + f)], ident[:])
                    last.then_inc(M["hturned"].sem, 1)

            pe.wait_ge(rt, R_DONE)
            for e in range(E):
                pe.wait_ge(experts_in[e], 32)
            turn_rows(0, 0)

            def three_tiles(t, first, last):
                before = None if first else expert_of(t * 3 - 1)
                for s in range(3):
                    j = t * 3 + s
                    own = expert_of(j)
                    up(j, own)
                    if before is not None:
                        down(j - 1, before)
                    if not (last and s == 2):
                        turn_rows(t + (s == 2), (s + 1) % 3)
                    turn_hidden(j)
                    before = own
                return before

            three_tiles(0, True, False)
            with pe.Fori(1, SLOTS // 3 - 1) as t:
                three_tiles(t, False, False)
            down(SLOTS - 1, three_tiles(SLOTS // 3 - 1, False, True))

        @block.scalar
        def _(act):
            act.wait_ge(weights_in, 16 * 4)
            act.wait_ge(tables_in, 16 * 10)

            def squash(g, half, _):
                for n in range(4):
                    ev["proj"].wait(act, g, n + 1)
                    dst, bias, m = (qT, bq, n) if n < 2 else (kT, bk, n - 2)
                    nc.scalar.activation(dst[:, m, :], BANK4[n][:], ACT.Sigmoid, bias=bias[:, m:m + 1])\
                        .then_inc(S["sig"], 1)

            def take_share1(g, half, _):
                ev["czt"].wait(act, g, 1)
                nc.scalar.activation(czT[:], pc[:, TURN:TURN + P], ACT.Copy).then_inc(S["cztc"], 1)

            def exps(g, half, _):
                ev["cons"].wait(act, g, 1)
                ev["clip"].wait(act, g, 1)
                nc.scalar.activation(ex[:, 0], cons[:, 0], ACT.Exp, scale=-1.0).then_inc(S["exps"], 1)
                nc.scalar.activation(ex[:, 1], cons[:, 1], ACT.Exp).then_inc(S["exps"], 1)

            def take_share2(g, half, _):
                ev["s3t"].wait(act, g, 1)
                nc.scalar.activation(s3T[:], pc[:, TURN:TURN + P], ACT.Copy).then_inc(S["s3tc"], 1)

            def take_k(g, half, c):
                ev["kt"].wait(act, g, c + 1)
                ev["upd"].wait(act, g, c - 1)
                nc.scalar.activation(ktok[:, c % 2, :], pm[:, 0:D], ACT.Copy).then_inc(S["ktc"], 1)

            def take_x(g, half, c):
                ev["av"].wait(act, g, c + 1)
                ev["wo"].wait(act, g, c - 1)
                nc.scalar.activation(two_flat(xat, c % 2), pm[:, 0:D], ACT.Copy).then_inc(S["xatc"], 1)

            def two_flat(tile, n):
                return tile[:, n].rearrange("p a b -> p (a b)")

            def take_h(g, half, _):
                for m in range(KT):
                    ev["h1t"].wait(act, g, m + 1)
                    nc.scalar.activation(h1T[:, m, :], pb[:], ACT.Copy).then_inc(S["h1tc"], 1)

            def gelu(g, half, f):
                if f == FT:
                    return
                ev["w1"].wait(act, g, f + 1)
                ev["w2"].wait(act, g, f - 1)
                nc.scalar.activation(hT[:, f % 2, :], pb[:], ACT.Gelu, bias=b1[:, f:f + 1])\
                    .then_inc(S["gelu"], 1)

            def take_row(g, half, c):
                ev["xn"].wait(act, g, c + 1)
                nc.scalar.activation(row(g, c), xn[:, c % 2], ACT.Copy).then_inc(S["xr"], 1)
                ev["xrt"].wait(act, g, c + 1)
                ev["lgm"].wait(act, g, c)
                nc.scalar.activation(xrT[:].rearrange("p a b -> p (a b)"), pb[:, 0:D], ACT.Copy)\
                    .then_inc(S["xrtc"], 1)

            all_groups(act, {"a_proj": squash, "a_dots1": take_share1, "a_dots2": exps, "a_comp": take_share2,
                             "a_pairs": take_k, "a_mix": take_x, "b_turn": take_h, "b_ffn": gelu,
                             "b_route": take_row})

            def take_rows(j):
                M["turned"].wait(act, j, 1)
                M["up"].wait(act, j - 1, 2)
                nc.scalar.activation(xsT[:].rearrange("p a b -> p (a b)"), pa[:, 0:D], ACT.Copy)\
                    .then_inc(M["xsT"].sem, 1)

            def hidden(j, last):
                M["up"].wait(act, j, 2)
                M["hturned"].wait(act, j - 1, 2)
                nc.scalar.activation(relu[:, 512:1024], ps1[:], ACT.Relu).then_inc(M["relu1"].sem, 1)
                if not last:
                    take_rows(j + 1)
                M["down"].wait(act, j - 1, 1)
                for n, src in enumerate((pm, pc)):
                    M["hturned"].wait(act, j, n + 1)
                    nc.scalar.activation(actT[:, 4 * n:4 * n + 4, :].rearrange("p f t -> p (f t)"), src[:],
                                         ACT.Square).then_inc(M["act"].sem, 1)

            take_rows(0)
            hidden(0, False)
            with act.Fori(1, SLOTS - 1) as j:
                hidden(j, False)
            hidden(SLOTS - 1, True)

        @block.gpsimd
        def _(pool):
            made = [0]

            def make(ins):
                made[0] += 1
                ins.then_inc(masks, 1)
                pool.wait_ge(masks, made[0])

            def keep_where(ap, op, base, pattern, fill=0.0):
                make(nc.gpsimd.affine_select(out=ap, in_=ap, compare_op=op, fill=fill, base=base,
                                             pattern=pattern, channel_multiplier=1))

            make(nc.gpsimd.memset(ident[:], 0.0))
            keep_where(ident[:], ALU.not_equal, 0, [[-1, P]], fill=1.0)
            make(nc.gpsimd.memset(ones[:], 1.0))
            make(nc.gpsimd.memset(ones_t[:], 1.0))
            make(nc.gpsimd.memset(minus_half[:], -0.5))
            make(nc.gpsimd.memset(upto[:], 0.0))
            keep_where(upto[:], ALU.is_gt, 0, [[-1, P]], fill=1.0)
            make(nc.gpsimd.memset(before[:], 0.0))
            keep_where(before[:], ALU.is_ge, 0, [[-1, P]], fill=1.0)
            for tile, inner in ((same_head, DH), (head_of, 1)):
                view = tile[:].rearrange("p (h d) -> p h d", d=inner)
                make(nc.gpsimd.memset(tile[:], 1.0))
                keep_where(view, ALU.is_ge, 0, [[-DH, HPT], [0, inner]])
                make(nc.gpsimd.affine_select(out=view, in_=view, compare_op=ALU.is_ge, fill=0.0, base=DH - 1,
                                             pattern=[[DH, HPT], [0, inner]], channel_multiplier=-1))
            make(nc.gpsimd.memset(share[:], 0.0))
            view = share[:].rearrange("p a m (h d) -> p a (m h) d", d=DH)
            keep_where(view, ALU.not_equal, 0, [[-H, 2 * NC], [-1, H], [0, DH]], fill=1.0)
            make(nc.gpsimd.iota(normal_i[:], [[P, L // P]], base=1, channel_multiplier=1))
            make(nc.gpsimd.tensor_copy(normal[:], normal_i[:]))
            make(nc.gpsimd.iota(early_i[:], [[1, E]], base=-E, channel_multiplier=0))
            make(nc.gpsimd.tensor_copy(early[:], early_i[:]))
            make(nc.gpsimd.iota(tile_at_i[:], [[P, SLOTS]], base=0, channel_multiplier=0))
            make(nc.gpsimd.tensor_copy(tile_at[:], tile_at_i[:]))
            make(nc.gpsimd.memset(vpad[:], 0.0))
            pool.sem_inc(masks_done, 1)
            make(nc.gpsimd.iota(xr[:].bitcast(I32)[:, :, D:ROW], [[P, NT], [0, ROW - D]], base=0,
                                channel_multiplier=1))
            make(nc.gpsimd.memset(empty[:, 0:D], 0.0))
            make(nc.gpsimd.memset(empty[:].bitcast(I32)[:, D:ROW], NO_TOKEN))
            pool.sem_inc(cleared, 1)
            pool.wait_ge(tables_in, 16 * 10)

            def add_bo(g, half, _):
                pool.wait_ge(x_in[half], (g - half) * 8 + 16)
                ev["r1"].wait(pool, g - 1, NC)
                nc.gpsimd.tensor_tensor(xb[:], x[:, half], bo[:].unsqueeze(1).broadcast_to([P, NC, D]), ALU.add)\
                    .then_inc(S["xb"], 1)

            def rsqrt(g, n, c):
                ev[f"ve{n + 1}"].wait(pool, g, c + 1)
                nc.gpsimd.tensor_tensor(rstd[:, n, c % 2], vare[:, n, c % 2], minus_half[:], ALU.pow)\
                    .then_inc(S[f"rs{n + 1}"], 1)

            def norm1(g, half, c):
                rsqrt(g, 0, c)
                ev["n1"].wait(pool, g, c + 1)
                ev["h1"].wait(pool, g, c - 1)
                nc.gpsimd.tensor_tensor(hg[:, c % 2], n1[:, c % 2], g1[:], ALU.mult).then_inc(S["hg"], 1)
                ev["hg"].wait(pool, g, c + 1)
                nc.gpsimd.tensor_tensor(h1[:, half, c], hg[:, c % 2], be1[:], ALU.add).then_inc(S["h1"], 1)
                ev["h1"].wait(pool, g, c + 1)
                nc.gpsimd.tensor_tensor(h1b[:, half, c], h1[:, half, c], b2[:], ALU.add).then_inc(S["h1b"], 1)

            def norm2(g, half, c):
                if c == NC:
                    rsqrt(g, 2, c - 1)
                    return
                rsqrt(g, 1, c)
                if c > 0:
                    rsqrt(g, 2, c - 1)
                ev["n2"].wait(pool, g, c + 1)
                ev["l2"].wait(pool, g, c - 1)
                nc.gpsimd.tensor_tensor(lg2[:, c % 2], n2[:, c % 2], g2[:], ALU.mult).then_inc(S["lg2"], 1)
                ev["lg2"].wait(pool, g, c + 1)
                ev["r3"].wait(pool, g, c - 1)
                nc.gpsimd.tensor_tensor(l2[:, c % 2], lg2[:, c % 2], be2[:], ALU.add).then_inc(S["l2"], 1)

            def spread_next(g, half, c):
                if c == 0:
                    spread_q(pool, 1, g, 0)
                if c + 1 < NC:
                    spread_q(pool, 1, g, c + 1)

            all_groups(pool, {"a_proj": add_bo, "a_pairs": spread_next, "a_mix": norm1, "b_tail": norm2})

            pool.wait_ge(rt, R_DONE)
            pool.wait_ge(gone, 16 * 3)
            for t in range(NT):
                nc.gpsimd.indirect_dma_start(
                    out=xs_d, out_offset=bass.IndirectOffsetOnAxis(ap=slot[:, t:t + 1], axis=0),
                    in_=xr[:, t, :], in_offset=None).then_inc(scattered, 16)

            def store(t, s):
                M["vare"].wait(pool, t * 3 + s, 1)
                nc.gpsimd.tensor_tensor(mrstd[:, s], mvare[:, s], minus_half[:], ALU.pow).then_inc(M["rstd"].sem, 1)
                M["y"].wait(pool, t * 3 + s, 1)
                apart(pool)
                nc.gpsimd.indirect_dma_start(
                    out=out_d, out_offset=bass.IndirectOffsetOnAxis(ap=xs[:].bitcast(I32)[:, s, D:D + 1], axis=0),
                    in_=y[:, s], in_offset=None, bounds_check=TOK - 1, oob_is_err=False).then_inc(y_out[s], 16)

            with pool.Fori(0, SLOTS // 3) as t:
                for s in range(3):
                    store(t, s)

        @block.vector
        def _(dve):
            dve.wait_ge(masks_done, 1)
            nc.vector.reciprocal(rnormal[:], normal[:]).then_inc(vector_ready, 1)
            dve.wait_ge(vector_ready, 1)
            dve.wait_ge(tables_in, 16 * 10)

            def scan(dst, src, start, done):
                nc.vector.tensor_tensor_scan(dst, ones_t[:], src, start, ALU.mult, ALU.add).then_inc(S[done], 1)

            def dot(w, other, done):
                flat = cc[:, w].rearrange("p m t -> p (m t)")
                nc.vector.scalar_tensor_tensor(flat, other[:].rearrange("p m t -> p (m t)"), EPS_FLOW, flat,
                                               ALU.add, ALU.mult).then_inc(S[done], 1)

            def begin(g, half, _):
                ev["sig"].wait(dve, g, 4)
                ev["upd"].wait(dve, g - 1, NC)
                for w in range(2):
                    for m in range(KT):
                        scan(cc[:, w, m], (kT, qT)[w][:, m], EPS_FLOW if half == 0 else
                             carry1[:, 2 * w + m:2 * w + m + 1], "scan1")
                ev["scan1"].wait(dve, g, 4)
                nc.vector.tensor_copy(carry1[:].unsqueeze(2), cc[:, :, :, T - 1:T].rearrange("p w m t -> p (w m) t"))\
                    .then_inc(S["carry1"], 1)
                ev["carry1"].wait(dve, g, 1)
                dot(0, qT, "dot1")
                dot(1, kT, "dot1")
                for n in range(2):
                    ev["proj"].wait(dve, g, 5 + n)
                    nc.vector.tensor_tensor(v[:, 2 * n:2 * n + 2, :],
                                            BANK4[n][:].rearrange("p (c d) -> p c d", c=2),
                                            bv[:].unsqueeze(1).broadcast_to([P, 2, D]), ALU.add)\
                        .then_inc(S["v"], 1)

            def normal_of(tile, half, lead):
                t = tile[:, half * NC:half * NC + NC]
                if lead:
                    return t.unsqueeze(1).unsqueeze(3).broadcast_to([P, lead, NC, H])
                return t.unsqueeze(2).broadcast_to([P, NC, H])

            def share1(g, half, _):
                ev["hs1"].wait(dve, g, 1)
                nc.vector.reciprocal(rden[:].rearrange("p w c h -> p (w c h)"), pc[:, SUMS:SUMS + 2 * NC * H])\
                    .then_inc(S["rden"], 1)
                ev["rden"].wait(dve, g, 1)
                nc.vector.tensor_tensor(cz[:], rden[:], normal_of(normal, half, 2), ALU.mult).then_inc(S["cz"], 1)

            def scaled(g, half, _):
                for n in range(4):
                    w, m = n // 2, n % 2
                    ev["bc1"].wait(dve, g, n + 1)
                    nc.vector.tensor_tensor(cc[:, 1 - w, m], BANK4[n][:], (qT, kT)[w][:, m], ALU.mult)\
                        .then_inc(S["scaled"], 1)
                ev["scaled"].wait(dve, g, 4)
                for w in range(2):
                    for m in range(KT):
                        scan(cc[:, w, m], cc[:, w, m], EPS_FLOW if half == 0 else
                             carry2[:, 2 * w + m:2 * w + m + 1], "scan2")
                ev["scan2"].wait(dve, g, 4)
                nc.vector.tensor_copy(carry2[:].unsqueeze(2), cc[:, :, :, T - 1:T].rearrange("p w m t -> p (w m) t"))\
                    .then_inc(S["carry2"], 1)
                ev["carry2"].wait(dve, g, 1)
                dot(0, qT, "dot2")
                dot(1, kT, "dot2")

            def conserve(g, half, _):
                ev["hs2"].wait(dve, g, 1)
                nc.vector.tensor_tensor(cons[:], pc[:, SUMS:SUMS + 2 * NC * H].rearrange(
                    "p (w c h) -> p w c h", w=2, c=NC), normal_of(rnormal, half, 2), ALU.mult)\
                    .then_inc(S["cons"], 1)
                ev["cons"].wait(dve, g, 1)
                nc.vector.tensor_scalar(cons[:, 1], cons[:, 1], 1.0, -1.0, ALU.min, ALU.max)\
                    .then_inc(S["clip"], 1)

            def scale_q(g, half, _):
                ev["exps"].wait(dve, g, 2)
                nc.vector.tensor_scalar(al0[:], ex[:, 0], 1.0, None, ALU.add).then_inc(S["al0"], 1)
                ev["al0"].wait(dve, g, 1)
                nc.vector.reciprocal(al1[:], al0[:]).then_inc(S["al1"], 1)
                ev["al1"].wait(dve, g, 1)
                ev["cum"].wait(dve, g, 1)
                sums = pc[:, UPTO:UPTO + NC * H].rearrange("p (c h) -> p c h", c=NC)
                if half == 0:
                    nc.vector.tensor_copy(csum[:], sums).then_inc(S["csum"], 1)
                else:
                    nc.vector.tensor_tensor(csum[:], sums, carry3[:].unsqueeze(1).broadcast_to([P, NC, H]),
                                            ALU.add).then_inc(S["csum"], 1)
                ev["csum"].wait(dve, g, 1)
                nc.vector.tensor_copy(carry3[:], pc[:, TOTAL:TOTAL + H]).then_inc(S["carry3"], 1)
                nc.vector.reciprocal(csr[:], csum[:]).then_inc(S["csr"], 1)
                ev["csr"].wait(dve, g, 1)
                nc.vector.tensor_tensor(comp0[:], ex[:, 1], csr[:], ALU.mult).then_inc(S["comp0"], 1)
                ev["comp0"].wait(dve, g, 1)
                nc.vector.tensor_tensor(cz2[:, 1], comp0[:], normal_of(normal, half, 0), ALU.mult)\
                    .then_inc(S["comp"], 1)
                ev["comp"].wait(dve, g, 1)
                nc.vector.tensor_tensor(cz2[:, 0], rden[:, 0], al1[:], ALU.mult).then_inc(S["s3"], 1)
                for c in range(NC):
                    nc.vector.tensor_tensor(
                        diag(c), v[:, c].rearrange("p (j e d) -> p j e d", e=2, d=DH),
                        cz2[:, 1, c].rearrange("p (j e) -> p j e", e=2).unsqueeze(3).broadcast_to(
                            [P, H // 2, 2, DH]), ALU.mult).then_inc(S["vp"], 1)

            def scaled_q(g, half, _):
                for m in range(KT):
                    ev["bc3"].wait(dve, g, m + 1)
                    nc.vector.tensor_tensor(cc[:, 0, m], BANK4[m][:], qT[:, m], ALU.mult).then_inc(S["qp"], 1)

            def pairs(g, half, c):
                if c == 0:
                    spread_q(dve, 0, g, 0)
                ev["av"].wait(dve, g, c)
                for n in range(4):
                    ev["s"].wait(dve, g, 4 * c + n + 1)
                    nc.vector.tensor_tensor(sm[:, n], (ps0, ps1)[n % 2][:].rearrange("p (h t) -> p h t", h=4),
                                            upto[:].unsqueeze(1).broadcast_to([P, 4, P]), ALU.mult)\
                        .then_inc(S["sm"], 1)
                if c + 1 < NC:
                    spread_q(dve, 0, g, c + 1)

            def norm(g, k, n, src, dst, c, done):
                nc.vector.bn_stats(bst[:, n, c % 2], src).then_inc(S[f"bs{n + 1}"], 1)
                ev[f"bs{n + 1}"].wait(dve, g, k)
                apart(dve)
                nc.vector.bn_aggr(mv[:, n, c % 2], bst[:, n, c % 2]).then_inc(S[f"ba{n + 1}"], 1)
                ev[f"ba{n + 1}"].wait(dve, g, k)
                nc.vector.tensor_scalar(vare[:, n, c % 2], mv[:, n, c % 2, 1:2], EPS_LN, None, ALU.add)\
                    .then_inc(S[f"ve{n + 1}"], 1)
                ev[f"rs{n + 1}"].wait(dve, g, k)
                nc.vector.tensor_scalar(dst, src, mv[:, n, c % 2, 0:1], rstd[:, n, c % 2], ALU.subtract, ALU.mult)\
                    .then_inc(S[done], 1)

            def mix(g, half, c):
                ev["upd"].wait(dve, g, c + 1)
                nc.vector.tensor_tensor(sttmp[:], ps0[:, 0:D].rearrange("p (m n) -> p m n", m=KT),
                                        same_head[:].unsqueeze(1).broadcast_to([P, KT, P]), ALU.mult)\
                    .then_inc(S["sttmp"], 1)
                ev["sttmp"].wait(dve, g, c + 1)
                if half == 0 and c == 0:
                    nc.vector.tensor_copy(state[:], sttmp[:]).then_inc(S["st"], 1)
                else:
                    nc.vector.tensor_tensor(state[:], state[:], sttmp[:], ALU.add).then_inc(S["st"], 1)
                ev["xb"].wait(dve, g, 1)
                ev["wo"].wait(dve, g, c + 1)
                nc.vector.tensor_tensor(r1[:, c % 2], pa[:, 0:D], xb[:, c], ALU.add)\
                    .then_inc(S["r1"], 1)
                ev["r1"].wait(dve, g, c + 1)
                ev["hg"].wait(dve, g, c - 1)
                norm(g, c + 1, 0, r1[:, c % 2], n1[:, c % 2], c, "n1")

            def tail(g, half, c):
                if c < NC:
                    ev["w2"].wait(dve, g, FT)
                    ev["h1b"].wait(dve, g, c + 1)
                    nc.vector.tensor_tensor(r2[:, c % 2], (po0, po1)[c // 2][:, (c % 2) * D:(c % 2) * D + D],
                                            h1b[:, half, c], ALU.add).then_inc(S["r2"], 1)
                    ev["r2"].wait(dve, g, c + 1)
                    ev["lg2"].wait(dve, g, c - 1)
                    norm(g, c + 1, 1, r2[:, c % 2], n2[:, c % 2], c, "n2")
                if c > 0:
                    d = c - 1
                    ev["l2"].wait(dve, g, d + 1)
                    nc.vector.tensor_tensor(r3[:, d % 2], l2[:, d % 2], x[:, half, d], ALU.add)\
                        .then_inc(S["r3"], 1)
                    ev["r3"].wait(dve, g, d + 1)
                    ev["xr"].wait(dve, g, d - 1)
                    ev["xrt"].wait(dve, g, d - 1)
                    norm(g, d + 1, 2, r3[:, d % 2], xn[:, d % 2], d, "xn")

            def take_logits(g, half, c):
                ev["lgm"].wait(dve, g, c + 1)
                at = logits[:, g * NC + c, :] if isinstance(g, int) else logits[:, bass.ds(g * NC + c, 1), :]\
                    .rearrange("p a e -> p (a e)")
                nc.vector.tensor_copy(at, pc[:, ROUTE:ROUTE + E])\
                    .then_inc(S["lg"], 1)

            all_groups(dve, {"a_proj": begin, "a_dots1": share1, "a_share1": scaled, "a_dots2": conserve,
                             "a_comp": scale_q, "a_share2": scaled_q, "a_pairs": pairs, "a_mix": mix,
                             "b_tail": tail, "b_logit": take_logits})

            steps = [0]

            def step(ins):
                steps[0] += 1
                ins.then_inc(rt, 1)
                dve.wait_ge(rt, steps[0])

            def over_e(tile):
                return tile[:].unsqueeze(2).broadcast_to([P, NT, E])

            def over_t(tile):
                return tile[:].unsqueeze(1).broadcast_to([P, NT, E])

            ev["lg"].wait(dve, G - 1, NC)
            ev["lgm"].wait(dve, G - 1, NC)
            step(nc.vector.tensor_reduce(best[:], logits[:], AX_X, ALU.max))
            step(nc.vector.tensor_tensor(hit[:], logits[:], over_e(best), ALU.is_equal))
            step(nc.vector.tensor_tensor(key[:], hit[:], over_t(early), ALU.mult))
            step(nc.vector.tensor_reduce(first[:], key[:], AX_X, ALU.min))
            step(nc.vector.tensor_tensor(onehot[:], over_t(early), over_e(first), ALU.is_equal))
            assert steps[0] == R_ONEHOT
            dve.wait_ge(sums_up, 1)
            step(nc.vector.tensor_copy(total[:].rearrange("p t e -> p (t e)"), ps0[:, 0:NT * E]))
            for e in range(E):
                step(nc.vector.tensor_tensor_scan(upto_tile[:, :, e], ones[:, 0:NT], total[:, :, e], 0.0,
                                                  ALU.mult, ALU.add))
            step(nc.vector.tensor_scalar(count_i[:], upto_tile[:, NT - 1, :], float(P - 1), None, ALU.add))
            step(nc.vector.tensor_scalar(count_i[:], count_i[:], 7, 7, ALU.arith_shift_right,
                                         ALU.logical_shift_left))
            step(nc.vector.tensor_copy(filled[:], count_i[:]))
            step(nc.vector.tensor_tensor_scan(end[:], ones[:, 0:E], filled[:], 0.0, ALU.mult, ALU.add))
            step(nc.vector.tensor_tensor(begin_at[:], end[:], filled[:], ALU.subtract))
            step(nc.vector.tensor_tensor(place[:], upto_tile[:], total[:], ALU.subtract))
            step(nc.vector.tensor_tensor(place[:], place[:], over_t(begin_at), ALU.add))
            step(nc.vector.tensor_tensor(place[:], pa[:, 0:NT * E].rearrange("p (t e) -> p t e", e=E), place[:],
                                         ALU.add))
            step(nc.vector.tensor_tensor(place_own[:], place[:], onehot[:], ALU.mult))
            step(nc.vector.tensor_reduce(slot_f[:], place_own[:], AX_X, ALU.add))
            step(nc.vector.tensor_copy(slot[:], slot_f[:]))
            step(nc.vector.tensor_tensor(passed[:], tile_at[:].unsqueeze(2).broadcast_to([P, SLOTS, E]),
                                         end[:].unsqueeze(1).broadcast_to([P, SLOTS, E]), ALU.is_ge))
            step(nc.vector.tensor_reduce(expert_f[:], passed[:], AX_X, ALU.add))
            step(nc.vector.tensor_scalar(expert[:], expert_f[:], float(E - 1), None, ALU.min))
            assert steps[0] == R_DONE

            def relu0(j):
                M["up"].wait(dve, j, 1)
                M["hturned"].wait(dve, j - 1, 1)
                nc.vector.tensor_scalar(relu[:, 0:512], ps0[:], 0.0, None, ALU.max).then_inc(M["relu0"].sem, 1)

            def finish(t, s):
                j = t * 3 + s
                M["down"].wait(dve, j, 1)
                dve.wait_ge(xs_in[s], t * 16 + 16)
                nc.vector.tensor_tensor(res[:, s], pb[:, 0:D], xs[:, s, 0:D], ALU.add).then_inc(M["res"].sem, 1)
                M["res"].wait(dve, j, 1)
                nc.vector.bn_stats(mst[:, s], res[:, s]).then_inc(M["stats"].sem, 1)
                M["stats"].wait(dve, j, 1)
                apart(dve)
                nc.vector.bn_aggr(mmv[:, s], mst[:, s]).then_inc(M["aggr"].sem, 1)
                M["aggr"].wait(dve, j, 1)
                nc.vector.tensor_scalar(mvare[:, s], mmv[:, s, 1:2], EPS_LN, None, ALU.add)\
                    .then_inc(M["vare"].sem, 1)
                M["rstd"].wait(dve, j, 1)
                if not isinstance(t, int) or t > 0:
                    dve.wait_ge(y_out[s], t * 16)
                nc.vector.tensor_scalar(y[:, s], res[:, s], mmv[:, s, 0:1], mrstd[:, s], ALU.subtract, ALU.mult)\
                    .then_inc(M["y"].sem, 1)

            relu0(0)
            for s in range(2):
                relu0(s + 1)
                finish(0, s)
            with dve.Fori(1, SLOTS // 3) as t:
                relu0(t * 3)
                finish(t - 1, 2)
                for s in range(2):
                    relu0(t * 3 + s + 1)
                    finish(t, s)
            finish(SLOTS // 3 - 1, 2)


R_ONEHOT = 5
R_DONE = R_ONEHOT + 1 + E + 11 + 3

_INS = ["x", "xT", "wqkvo", "bq", "bk", "bv", "bo", "g1", "be1", "w1", "b1", "w2", "b2", "g2", "be2", "rw", "fc", "pj"]


def kernel(**inputs):
    import numpy as np
    import concourse.bacc as bacc
    from concourse.bass_utils import run_bass_kernel_spmd as run

    a = {k: np.asarray(v) for k, v in inputs.items()}
    rows = a["L0_attn_inputs"].reshape(TOK, D)

    def columns(vector):
        return vector.reshape(-1, P).T

    laid = {
        "x": rows.reshape(NT, P, D).transpose(1, 0, 2),
        "xT": rows.T.reshape(KT, P, TOK).transpose(1, 0, 2),
        "wqkvo": np.stack([a[f"L0_attn_W{n}"] for n in "qkvo"]),
        "bq": columns(a["L0_attn_bq"]), "bk": columns(a["L0_attn_bk"]),
        "bv": a["L0_attn_bv"], "bo": a["L0_attn_bo"],
        "g1": a["L0_attn_ln1_g"], "be1": a["L0_attn_ln1_b"],
        "w1": a["L0_attn_W1"], "b1": columns(a["L0_attn_b1"]), "w2": a["L0_attn_W2"], "b2": a["L0_attn_b2"],
        "g2": a["L0_attn_ln2_g"], "be2": a["L0_attn_ln2_b"],
        "rw": a["L0_ffn_router_w"].T, "fc": a["L0_ffn_expert_fc"],
        "pj": a["L0_ffn_expert_proj"].transpose(0, 2, 1),
    }
    nc = bacc.Bacc("TRN2", target_bir_lowering=False, num_devices=1)
    arrays = {f"in_{n}": np.ascontiguousarray(laid[n]) for n in _INS}
    args = [nc.dram_tensor(n, arrays[n].shape, mybir.dt.from_np(arrays[n].dtype), kind="ExternalInput").ap()
            for n in arrays]
    out = nc.dram_tensor("out_rows", [TOK, D], F32, kind="ExternalOutput").ap()
    build(nc, *args, out)
    r = run(nc, [arrays], core_ids=[0])
    return r.results[0]["out_rows"].reshape(B, L, D)
```
